# Optimizing a Trainium2 kernel written in Bass

```python
import numpy as np
import jax
import jax.numpy as jnp

def _softmax(x, axis=-1):
    return jax.nn.softmax(x, axis=axis)

def _gelu(x):
    return jax.nn.gelu(x, approximate=True)

def _silu(x):
    return jax.nn.silu(x)

def _sigmoid(x):
    return jax.nn.sigmoid(x)

def _layernorm(x, axis=-1, eps=1e-05):
    m = jnp.mean(x, axis=axis, keepdims=True)
    v = jnp.var(x, axis=axis, keepdims=True)
    return (x - m) / jnp.sqrt(v + eps)

def _scatter_add(tgt, idx, src, axis=0):
    return tgt.at[idx].add(src)

def _segment_sum(src, seg, n):
    return jax.ops.segment_sum(src, seg, n)
kernel_name = 'mk_adj_preln_d1_adj_r2_491e4d'

def setup_inputs(seed: int=0):
    np.random.seed(seed)
    _w = jnp.asarray

    def _rec_inputs():
        import jax
        import jax.numpy as jnp
        _gk = jax.random.key(seed)
        x = -8.776e-05 + 1 * jax.random.normal(jax.random.fold_in(_gk, 1), (10000, 128), jnp.float32)
        _w = (1.0 + jnp.arange(10000, dtype=jnp.float32)) ** (-0.5)
        _w = _w / _w.mean()
        _pij = jnp.clip(0.0016 * _w[:, None] * _w[None, :], 0.0, 1.0)
        _a = jax.random.uniform(jax.random.fold_in(_gk, 2), (10000, 10000)) < _pij
        _a = jnp.logical_or(_a, jnp.eye(10000, dtype=bool))
        _af = _a.astype(jnp.float32)
        _af = _af * jax.random.uniform(jax.random.fold_in(_gk, 3), (10000, 10000), jnp.float32, 0.05, 1)
        adj = _af
        return (x, adj)
    x, adj = _rec_inputs()

    def _L0_gnn_setup():
        import jax, jax.numpy as jnp
        import numpy as np
        N_USER = 10000
        N_ITEM = 10000
        HID = 128
        key = jax.random.key(seed)
        k1, k2, k3, k4, k5, k6, k7 = jax.random.split(key, 7)
        scale = 1.0 / np.sqrt(HID)
        return {'user_feat': jax.random.normal(k1, (N_USER, HID), dtype=jnp.float32), 'item_feat': jax.random.normal(k2, (N_ITEM, HID), dtype=jnp.float32), 'adj': jax.random.uniform(k3, (N_USER, N_ITEM), dtype=jnp.float32), 'W_item': jax.random.uniform(k4, (HID, HID), dtype=jnp.float32, minval=-scale, maxval=scale), 'b_item': jax.random.uniform(k5, (HID,), dtype=jnp.float32, minval=-scale, maxval=scale), 'W_user': jax.random.uniform(k6, (HID, HID), dtype=jnp.float32, minval=-scale, maxval=scale), 'b_user': jax.random.uniform(k7, (HID,), dtype=jnp.float32, minval=-scale, maxval=scale)}
    _L0_gnn_all = _L0_gnn_setup()
    _L0_gnn_in = {k: v for k, v in _L0_gnn_all.items() if k in ('item_feat', 'W_item', 'b_item', 'W_user', 'b_user')}
    del _L0_gnn_all
    return {'x': x, 'adj': adj, 'L0_gnn_item_feat': _L0_gnn_in['item_feat'], 'L0_gnn_W_item': _L0_gnn_in['W_item'], 'L0_gnn_b_item': _L0_gnn_in['b_item'], 'L0_gnn_W_user': _L0_gnn_in['W_user'], 'L0_gnn_b_user': _L0_gnn_in['b_user']}

def reference(x, adj, L0_gnn_item_feat, L0_gnn_W_item, L0_gnn_b_item, L0_gnn_W_user, L0_gnn_b_user):
    import jax
    import jax.numpy as jnp

    def _L0_gnn_ref(user_feat, item_feat, adj, W_item, b_item, W_user, b_user):
        import jax, jax.numpy as jnp
        import numpy as np
        N_USER = 10000
        N_ITEM = 10000
        HID = 128
        h = item_feat @ W_item.T + b_item
        b = user_feat @ W_user.T + b_user
        return jax.nn.relu(adj @ h + b)
    h = jnp.maximum(_layernorm(x, axis=-1), 0.0)
    x = x + _L0_gnn_ref(h, L0_gnn_item_feat, adj, L0_gnn_W_item, L0_gnn_b_item, L0_gnn_W_user, L0_gnn_b_user)
    return x

_drawn_inputs = setup_inputs


def setup_inputs(seed=0):
    import zlib

    import numpy as np

    out = dict(_drawn_inputs(seed))
    spreads = {}
    factors = {}
    for name, (base, spread) in spreads.items():
        noise = np.random.default_rng([zlib.crc32(name.encode()), seed]).standard_normal(out[name].shape)
        drawn = base * np.exp(spread * noise) if base else spread * noise
        out[name] = jnp.asarray(drawn.astype(out[name].dtype))
    for name, factor in factors.items():
        out[name] = (out[name] * factor).astype(out[name].dtype)
    return out
```

```python
from contextlib import ExitStack

import concourse.bass as bass
from concourse import mybir

P = 128
HID = 128
N_USER = 10000
N_ITEM = 10000
BANK = 500
BANKS = 4
BLOCK = BANK * BANKS
BLOCKS = N_USER // BLOCK
CHUNKS = BLOCKS * BANKS
TILES = N_ITEM // P
TAIL = N_ITEM - TILES * P
STACK = 4 * TAIL
A_SLOTS = 6
PART_SLOTS = 3
XG = 4
HC = 3
H_CHUNKS = TILES // HC
ITEM_COLS = TILES * P + STACK
SECTION = 3 * A_SLOTS
EPS = 1e-5

F32 = mybir.dt.float32
F32R = mybir.dt.float32r
ALU = mybir.AluOpType
ACT = mybir.ActivationFunctionType

assert BLOCKS * BLOCK == N_USER and TILES % A_SLOTS == 0 and TILES % PART_SLOTS == 0
assert TILES == A_SLOTS + BANKS * SECTION and H_CHUNKS % 2 == 0
assert A_SLOTS * BLOCK >= ITEM_COLS and STACK == P // 2


def build(nc, adj_main, adj_tail, x_rows, x_cols, item_cols, w_item_t, w_user_t, b_item_rows, b_user_rows,
          identity, split_masks, out):
    ctx = ExitStack()
    with ctx:
        def sb(name, shape, dt=F32):
            return ctx.enter_context(nc.sbuf_tensor(name, shape, dt))

        def sem(name):
            return ctx.enter_context(nc.semaphore(name))

        a_ring = sb("a_ring", [P, A_SLOTS * BLOCK])
        high_ring = sb("high_ring", [P, PART_SLOTS * BLOCK], F32R)
        low_ring = sb("low_ring", [P, PART_SLOTS * BLOCK], F32R)
        h_high = sb("h_high", [P, TILES * HID], F32R)
        h_low = sb("h_low", [P, TILES * HID], F32R)
        h_sum = sb("h_sum", [P, 2, HC * HID])
        tail_h = sb("tail_h", [P, HID])
        tail_weights = sb("tail_weights", [P, HID], F32R)
        tail_raw = sb("tail_raw", [P, 2, BANK])
        tail_moving = sb("tail_moving", [P, 2, BANK], F32R)
        xr = sb("xr", [P, 2, XG * HID])
        user_t = sb("user_t", [P, 2, XG * P])
        xo = sb("xo", [P, BLOCK])
        w_item = sb("w_item", [P, HID])
        w_user = sb("w_user", [P, HID])
        b_item = sb("b_item", [P, HID])
        ident = sb("ident", [P, P])
        masks = sb("masks", [P, 2])
        eps = sb("eps", [P, 1])
        stats = sb("stats", [P, XG, 6])
        mean_var = sb("mean_var", [P, XG, 2])
        std = sb("std", [P, XG])
        rstd = sb("rstd", [P, XG])

        sums = [ctx.enter_context(nc.psum_tensor(f"sums{b}", [P, 512], F32)) for b in range(BANKS)]
        xt_ps = [ctx.enter_context(nc.psum_tensor(f"xt_ps{e}", [P, 512], F32)) for e in range(2)]
        h_ps = [ctx.enter_context(nc.psum_tensor(f"h_ps{e}", [P, 512], F32)) for e in range(2)]

        consts_in = sem("consts_in")
        item_in = [sem(f"item_in{s}") for s in range(A_SLOTS)]
        a_in = [sem(f"a_in{s}") for s in range(A_SLOTS)]
        xr_in = [sem(f"xr_in{e}") for e in range(2)]
        tail_in = [sem(f"tail_in{e}") for e in range(2)]
        x_cols_in = sem("x_cols_in")
        out_stored = sem("out_stored")
        h_multiplied = sem("h_multiplied")
        h_summed = sem("h_summed")
        h_high_done = sem("h_high_done")
        h_low_done = sem("h_low_done")
        ready = sem("ready")
        high_done = sem("high_done")
        low_done = sem("low_done")
        tile_used = sem("tile_used")
        bank_done = sem("bank_done")
        bank_free = [sem(f"bank_free{b}") for b in range(BANKS)]
        stats_done = sem("stats_done")
        moments_done = sem("moments_done")
        std_done = sem("std_done")
        rstd_done = sem("rstd_done")
        x_normal = sem("x_normal")
        xt_done = [sem(f"xt_done{e}") for e in range(2)]
        user_done = sem("user_done")
        tail_high_done = sem("tail_high_done")
        tail_done = [sem(f"tail_done{e}") for e in range(2)]
        tail_used = [sem(f"tail_used{e}") for e in range(2)]

        CONSTS = 6
        block = ctx.enter_context(nc.Block())

        def a_slot(s):
            return a_ring[:, s * BLOCK:(s + 1) * BLOCK]

        def part(ring, s):
            return ring[:, s * BLOCK:(s + 1) * BLOCK]

        def item_slot_cols(s):
            return min(BLOCK, ITEM_COLS - s * BLOCK)

        @block.sync
        def _(sp):
            sp.dma_start(w_item[:, :], w_item_t).then_inc(consts_in, 16)
            sp.dma_start(b_item[:, :], b_item_rows).then_inc(consts_in, 16)
            for s in range(A_SLOTS):
                n = item_slot_cols(s)
                sp.dma_start(a_ring[:, s * BLOCK:s * BLOCK + n],
                             item_cols[:, s * BLOCK:s * BLOCK + n]).then_inc(item_in[s], 16)
            sp.dma_start(w_user[:, :], w_user_t).then_inc(consts_in, 16)
            sp.dma_start(ident[:, :], identity).then_inc(consts_in, 16)
            sp.dma_start(masks[:, :], split_masks).then_inc(consts_in, 16)
            sp.dma_start(tail_h[STACK:P, :], b_user_rows).then_inc(consts_in, 16)

            def load_tile(tile, s):
                sp.dma_start(a_slot(s), adj_main[bass.ds(tile * P, P), :]).then_inc(a_in[s], 16)

            def load_tiles(tile, groups):
                with sp.Fori(0, groups) as k:
                    for s in range(A_SLOTS):
                        sp.wait_ge(low_done, tile + k * A_SLOTS + (s - A_SLOTS + 1))
                        load_tile(tile + k * A_SLOTS + s, s)

            def load_block(n):
                first = TILES * n
                if isinstance(n, int):
                    for s in range(A_SLOTS):
                        last_tile = min(TILES, ((s + 1) * BLOCK - 1) // P)
                        sp.wait_ge(h_multiplied, last_tile // HC + 1)
                        load_tile(s, s)
                else:
                    load_tiles(first, 1)
                for q in range(BANKS):
                    e, use = q % 2, 2 * n + q // 2
                    reused = not isinstance(n, int) or use > 0
                    if reused:
                        sp.wait_ge(xt_done[e], use)
                    sp.dma_start(xr[:, e, :], x_rows[bass.ds((n * BANKS + q) * P, P), :]).then_inc(xr_in[e], 16)
                    if reused:
                        sp.wait_ge(tail_done[e], use)
                    sp.dma_start(tail_raw[0:STACK, e, :],
                                 adj_tail[bass.ds((n * BANKS + q) * STACK, STACK), :]).then_inc(tail_in[e], 16)
                    if q == 1 and not isinstance(n, int):
                        sp.wait_ge(bank_free[BANKS - 1], n)
                        sp.dma_start(out[bass.ds((n - 1) * P, P), :], xo[:, :]).then_inc(out_stored, 16)
                    if q == 2:
                        if not isinstance(n, int):
                            sp.wait_ge(out_stored, n * 16)
                        sp.dma_start(xo[:, :], x_cols[bass.ds(n * P, P), :]).then_inc(x_cols_in, 16)
                    load_tiles(first + A_SLOTS + q * SECTION, SECTION // A_SLOTS)

            load_block(0)
            with sp.Fori(1, BLOCKS) as n:
                load_block(n)
            for b in range(BANKS):
                sp.wait_ge(bank_free[b], BLOCKS)
                sp.dma_start(out[(BLOCKS - 1) * P:BLOCKS * P, b * BANK:(b + 1) * BANK],
                             xo[:, b * BANK:(b + 1) * BANK]).then_inc(out_stored, 16)
            sp.wait_ge(out_stored, (BLOCKS - 1 + BANKS) * 16)

        @block.scalar
        def _(act):
            def h_high_part(c, e):
                act.wait_ge(h_summed, c + 1)
                nc.scalar.activation(h_high[:, bass.ts(c, HC * HID)], h_sum[:, e, :],
                                     ACT.Copy).then_inc(h_high_done, 1)

            with act.Fori(0, H_CHUNKS // 2) as i:
                for e in range(2):
                    h_high_part(2 * i + e, e)
            act.wait_ge(consts_in, CONSTS * 16)
            act.wait_ge(h_summed, H_CHUNKS + 1)
            nc.scalar.activation(tail_weights[:, :], tail_h[:, :], ACT.Copy).then_inc(h_high_done, 1)

            def high_tile(loads, used, s, r):
                act.wait_ge(a_in[s], loads * 16)
                if used is not None:
                    act.wait_ge(tile_used, used)
                nc.scalar.activation(part(high_ring, r), a_slot(s), ACT.Copy).then_inc(high_done, 1)

            def high_sections(n, half, reused):
                for e in range(2):
                    use = 2 * n + half
                    chunk = BANKS * n + 2 * half + e
                    tiles = TILES * n + 2 * SECTION * half + (A_SLOTS + e * SECTION)
                    group = (TILES // A_SLOTS) * n + 6 * half + (1 + e * 3)

                    def some(j0):
                        for j in range(j0, j0 + A_SLOTS):
                            high_tile(group + (j // A_SLOTS + 1), tiles + (j - PART_SLOTS + 1),
                                      j % A_SLOTS, j % PART_SLOTS)

                    act.wait_ge(tail_in[e], (use + 1) * 16)
                    if reused:
                        act.wait_ge(tail_used[e], use)
                    nc.scalar.activation(tail_moving[0:STACK, e, :], tail_raw[0:STACK, e, :],
                                         ACT.Copy).then_inc(tail_high_done, 1)
                    some(0)
                    act.wait_ge(moments_done, chunk + 1)
                    nc.scalar.activation(std[:, :], mean_var[:, :, 1], ACT.Sqrt,
                                         bias=eps[:, 0:1]).then_inc(std_done, 1)
                    some(A_SLOTS)
                    act.wait_ge(xt_done[e], use + 1)
                    nc.scalar.activation(user_t[:, e, :], xt_ps[e][:, :], ACT.Relu).then_inc(user_done, 1)
                    some(2 * A_SLOTS)

            def high_block(n, first=False):
                for j in range(A_SLOTS):
                    used = None if first and j < PART_SLOTS else n * TILES + (j - PART_SLOTS + 1)
                    high_tile(n * (TILES // A_SLOTS) + 1, used, j, j % PART_SLOTS)
                if first:
                    for half in range(BANKS // 2):
                        high_sections(n, half, half > 0)
                else:
                    with act.Fori(0, BANKS // 2) as half:
                        high_sections(n, half, True)

            act.wait_ge(ready, 1)
            high_block(0, first=True)
            with act.Fori(1, BLOCKS) as n:
                high_block(n)

        @block.vector
        def _(dve):
            dve.wait_ge(consts_in, CONSTS * 16)
            nc.vector.memset(eps[:, :], EPS)
            nc.vector.memset(tail_moving[STACK:P, :, :].bitcast(F32), 1.0).then_inc(ready, 1)

            b_wide = b_item[:, :].unsqueeze(1).to_broadcast([P, HC, HID])

            def add_bias(c, e, first=False):
                if not first:
                    dve.wait_ge(h_low_done, c - 1)
                dve.wait_ge(h_multiplied, c + 1)
                nc.vector.tensor_tensor(h_sum[:, e, :].rearrange("p (t h) -> p t h", t=HC),
                                        h_ps[e][:, 0:HC * HID].rearrange("p (t h) -> p t h", t=HC),
                                        b_wide, ALU.add).then_inc(h_summed, 1)

            def h_low_part(c, e):
                dve.wait_ge(h_high_done, c + 1)
                nc.vector.tensor_tensor(h_low[:, bass.ts(c, HC * HID)], h_sum[:, e, :],
                                        h_high[:, bass.ts(c, HC * HID)].bitcast(F32),
                                        ALU.subtract).then_inc(h_low_done, 1)

            add_bias(0, 0, first=True)
            add_bias(1, 1, first=True)
            with dve.Fori(0, H_CHUNKS // 2 - 1) as i:
                for e in range(2):
                    h_low_part(2 * i + e, e)
                    add_bias(2 * i + (e + 2), e)
            h_low_part(H_CHUNKS - 2, 0)
            dve.wait_ge(h_multiplied, H_CHUNKS + 1)
            nc.vector.tensor_tensor(tail_h[0:STACK, :], h_ps[0][0:STACK, 0:HID], b_item[0:STACK, :],
                                    ALU.add).then_inc(h_summed, 1)
            h_low_part(H_CHUNKS - 1, 1)
            dve.wait_ge(h_high_done, H_CHUNKS + 1)
            nc.vector.scalar_tensor_tensor(out=tail_weights[:, :], in0=tail_weights[:, :].bitcast(F32),
                                           scalar=masks[:, 1:2], in1=tail_h[:, :], op0=ALU.mult,
                                           op1=ALU.add).then_inc(ready, 1)

            def low_tile(done, s, r):
                dve.wait_ge(high_done, done)
                nc.vector.tensor_tensor(part(low_ring, r), a_slot(s), part(high_ring, r).bitcast(F32),
                                        ALU.subtract).then_inc(low_done, 1)

            def finish_bank(n, b):
                if b < BANKS - 1:
                    dve.wait_ge(bank_done, n * (BANKS - 1) + (b - BANKS + 2))
                else:
                    dve.wait_ge(tile_used, n * TILES)
                dve.wait_ge(x_cols_in, n * 16)
                nc.vector.scalar_tensor_tensor(out=xo[:, b * BANK:(b + 1) * BANK], in0=sums[b][:, 0:BANK],
                                               scalar=0.0, in1=xo[:, b * BANK:(b + 1) * BANK], op0=ALU.max,
                                               op1=ALU.add).then_inc(bank_free[b], 1)

            def low_block(n, first=False):
                for j in range(A_SLOTS):
                    low_tile(n * TILES + (j + 1), j, j % PART_SLOTS)
                    if j == 1 and not first:
                        for b in range(BANKS):
                            finish_bank(n, b)
                with dve.Fori(0, BANKS // 2) as half:
                    for e in range(2):
                        use = 2 * n + half
                        chunk = BANKS * n + 2 * half + e
                        tiles = TILES * n + 2 * SECTION * half + (A_SLOTS + e * SECTION)

                        def some(start, end):
                            for j in range(start, end):
                                low_tile(tiles + (j + 1), j % A_SLOTS, j % PART_SLOTS)

                        dve.wait_ge(xr_in[e], (use + 1) * 16)
                        for g in range(XG):
                            last = nc.vector.bn_stats(stats[:, g, :], xr[:, e, g * HID:(g + 1) * HID])
                        last.then_inc(stats_done, 1)
                        dve.wait_ge(stats_done, chunk + 1)
                        some(0, 1)
                        for g in range(XG):
                            last = nc.vector.bn_aggr(mean_var[:, g, :], stats[:, g, :])
                        last.then_inc(moments_done, 1)
                        some(1, A_SLOTS)
                        dve.wait_ge(std_done, chunk + 1)
                        nc.vector.reciprocal(rstd[:, :], std[:, :]).then_inc(rstd_done, 1)
                        dve.wait_ge(rstd_done, chunk + 1)
                        for g in range(XG):
                            rows = xr[:, e, g * HID:(g + 1) * HID]
                            last = nc.vector.tensor_scalar(rows, rows, mean_var[:, g, 0:1], rstd[:, g:g + 1],
                                                           ALU.subtract, ALU.mult)
                        last.then_inc(x_normal, 1)
                        dve.wait_ge(tail_high_done, chunk + 1)
                        nc.vector.scalar_tensor_tensor(out=tail_moving[0:STACK, e, :],
                                                       in0=tail_moving[0:STACK, e, :].bitcast(F32),
                                                       scalar=masks[0:STACK, 0:1], in1=tail_raw[0:STACK, e, :],
                                                       op0=ALU.mult, op1=ALU.add).then_inc(tail_done[e], 1)
                        some(A_SLOTS, 2 * A_SLOTS)
                        some(2 * A_SLOTS, SECTION)

            low_block(0, first=True)
            with dve.Fori(1, BLOCKS) as n:
                low_block(n)
            for b in range(BANKS):
                finish_bank(BLOCKS, b)

        @block.tensor
        def _(pe):
            pe.wait_ge(consts_in, CONSTS * 16)
            for c in range(H_CHUNKS + 1):
                if c >= 2:
                    pe.wait_ge(h_summed, c - 1)
                for k in range(HC if c < H_CHUNKS else 1):
                    t = c * HC + k
                    m = P if t < TILES else STACK
                    for s in range(A_SLOTS):
                        if t * P <= s * BLOCK < t * P + m or (t == 0 and s == 0):
                            pe.wait_ge(item_in[s], 16)
                    last = nc.tensor.matmul(h_ps[c % 2][0:m, k * HID:(k + 1) * HID],
                                            a_ring[:, t * P:t * P + m], w_item[:, :], start=True, stop=True)
                last.then_inc(h_multiplied, 1)
            pe.wait_ge(h_low_done, H_CHUNKS)
            pe.wait_ge(ready, 2)

            def product(t, weights, ring, b, start=False, stop=False):
                r = t % PART_SLOTS
                return nc.tensor.matmul(sums[b][:, 0:BANK], weights[:, t * HID:(t + 1) * HID],
                                        ring[:, r * BLOCK + b * BANK:r * BLOCK + (b + 1) * BANK],
                                        start=start, stop=stop)

            def multiply_block(n, first=False):
                for t in range(TILES):
                    section, at = divmod(t - A_SLOTS, SECTION)
                    q, e = section, section % 2
                    if section >= 0 and at == A_SLOTS:
                        pe.wait_ge(x_normal, n * BANKS + (q + 1))
                        for g in range(XG):
                            last = nc.tensor.transpose(xt_ps[e][:, g * P:(g + 1) * P],
                                                       xr[:, e, g * HID:(g + 1) * HID], ident[:, :])
                        last.then_inc(xt_done[e], 1)
                    if section >= 0 and at == 2 * A_SLOTS + PART_SLOTS:
                        pe.wait_ge(user_done, n * BANKS + (q + 1))
                        nc.tensor.matmul(sums[q][:, 0:BANK], w_user[:, :], user_t[:, e, 0:BANK],
                                         start=False, stop=False)
                        pe.wait_ge(tail_done[e], n * 2 + (q // 2 + 1))
                        nc.tensor.matmul(sums[q][:, 0:BANK], tail_weights[:, :], tail_moving[:, e, :],
                                         start=False, stop=False).then_inc(tail_used[e], 1)
                    pe.wait_ge(low_done, n * TILES + (t + 1))
                    if t < TILES - 1:
                        for b in range(BANKS):
                            if t == 0 and not first:
                                pe.wait_ge(bank_free[b], n)
                            product(t, h_high, high_ring, b, start=(t == 0))
                        for b in range(BANKS):
                            product(t, h_high, low_ring, b)
                        for b in range(BANKS):
                            last = product(t, h_low, high_ring, b)
                        last.then_inc(tile_used, 1)
                    else:
                        for b in range(BANKS):
                            product(t, h_high, high_ring, b)
                            product(t, h_high, low_ring, b)
                            last = product(t, h_low, high_ring, b, stop=True)
                            last.then_inc(bank_done if b < BANKS - 1 else tile_used, 1)

            multiply_block(0, first=True)
            with pe.Fori(1, BLOCKS) as n:
                multiply_block(n)


def kernel(x, adj, L0_gnn_item_feat, L0_gnn_W_item, L0_gnn_b_item, L0_gnn_W_user, L0_gnn_b_user):
    import numpy as np
    import concourse.bacc as bacc
    from concourse.bass_utils import run_bass_kernel_spmd

    f = np.float32
    x, adj, item, wi, bi, wu, bu = (np.asarray(a) for a in (
        x, adj, L0_gnn_item_feat, L0_gnn_W_item, L0_gnn_b_item, L0_gnn_W_user, L0_gnn_b_user))
    whole = TILES * P
    adj_t = adj.T
    adj_main = np.empty((BLOCKS, TILES, P, BLOCK), f)
    for n in range(BLOCKS):
        adj_main[n] = adj_t[:whole, n * BLOCK:(n + 1) * BLOCK].reshape(TILES, P, BLOCK)
    adj_tail = np.tile(adj_t[whole:].reshape(TAIL, CHUNKS, BANK).transpose(1, 0, 2), (1, 4, 1))
    rows = np.zeros((CHUNKS, XG * P, HID), f)
    rows[:, :BANK] = x.reshape(CHUNKS, BANK, HID)
    bias_rows = np.zeros((P - STACK, HID), f)
    bias_rows[0:2] = bu
    masks = np.zeros((P, 2), f)
    masks[TAIL:2 * TAIL, 0] = masks[3 * TAIL:4 * TAIL, 0] = -1
    masks[2 * TAIL:4 * TAIL, 1] = masks[STACK + 1, 1] = -1
    arrays = {
        "adj_main": adj_main.reshape(BLOCKS * TILES * P, BLOCK),
        "adj_tail": adj_tail.reshape(CHUNKS * STACK, BANK),
        "x_rows": rows.reshape(CHUNKS, XG, P, HID).transpose(0, 2, 1, 3).reshape(CHUNKS * P, XG * HID),
        "x_cols": x.T.reshape(HID, BLOCKS, BLOCK).transpose(1, 0, 2).reshape(BLOCKS * HID, BLOCK),
        "item_cols": np.concatenate([item.T[:, :whole]] + [item.T[:, whole:]] * 4, axis=1),
        "w_item_t": wi.T, "w_user_t": wu.T,
        "b_item_rows": np.tile(bi, (P, 1)), "b_user_rows": bias_rows,
        "identity": np.eye(P, dtype=f), "split_masks": masks,
    }
    arrays = {k: np.ascontiguousarray(v) for k, v in arrays.items()}
    nc = bacc.Bacc("TRN2", target_bir_lowering=False, num_devices=1)
    args = [nc.dram_tensor(k, v.shape, mybir.dt.from_np(v.dtype), kind="ExternalInput").ap()
            for k, v in arrays.items()]
    out = nc.dram_tensor("out", (BLOCKS * HID, BLOCK), F32, kind="ExternalOutput").ap()
    build(nc, *args, out)
    r = run_bass_kernel_spmd(nc, [arrays], core_ids=[0])
    return np.ascontiguousarray(
        r.results[0]["out"].reshape(BLOCKS, HID, BLOCK).transpose(0, 2, 1).reshape(N_USER, HID))
```

```python
from contextlib import ExitStack

import concourse.bass as bass
from concourse import mybir

P = 128
HID = 128
N_USER = 10000
N_ITEM = 10000
BANK = 500
BANKS = 4
BLOCK = BANK * BANKS
BLOCKS = N_USER // BLOCK
CHUNKS = BLOCKS * BANKS
TILES = N_ITEM // P
TAIL = N_ITEM - TILES * P
STACK = (0, 32, 64, 96)
BIAS = 96 + TAIL
A_SLOTS = 6
PART_SLOTS = 3
XG = 4
HC = 3
H_CHUNKS = TILES // HC
SECTION = 3 * A_SLOTS
EPS = 1e-5

F32 = mybir.dt.float32
F32R = mybir.dt.float32r
ALU = mybir.AluOpType
ACT = mybir.ActivationFunctionType

assert BLOCKS * BLOCK == N_USER and TILES % A_SLOTS == 0 and TILES % PART_SLOTS == 0
assert TILES == A_SLOTS + BANKS * SECTION and H_CHUNKS % 2 == 0
assert TAIL <= 32 and BIAS + 2 <= P


def build(nc, adj_main, adj_tail, x_rows, item_cols, item_tail_cols, w_item_t, w_user_t, b_item_rows,
          b_tail_rows, identity, split_mask, out):
    ctx = ExitStack()
    with ctx:
        def sb(name, shape, dt=F32):
            return ctx.enter_context(nc.sbuf_tensor(name, shape, dt))

        def sem(name):
            return ctx.enter_context(nc.semaphore(name))

        a_ring = sb("a_ring", [P, A_SLOTS * BLOCK])
        high_ring = sb("high_ring", [P, PART_SLOTS * BLOCK], F32R)
        low_ring = sb("low_ring", [P, PART_SLOTS * BLOCK], F32R)
        h_high = sb("h_high", [P, TILES * HID], F32R)
        h_low = sb("h_low", [P, TILES * HID], F32R)
        item_t = sb("item_t", [P, 2, HC * P])
        item_tail_t = sb("item_tail_t", [P, P])
        h_sum = sb("h_sum", [P, 2, HC * HID])
        tail_sum = sb("tail_sum", [P, HID])
        tail_weights = sb("tail_weights", [P, HID], F32R)
        tail_raw = sb("tail_raw", [TAIL, 2, BANK])
        tail_moving = sb("tail_moving", [P, 2, BANK], F32R)
        xr = sb("xr", [P, 2, XG * HID])
        user_t = sb("user_t", [P, 2, XG * P])
        xo = sb("xo", [P, BLOCK])
        w_item = sb("w_item", [P, HID])
        w_user = sb("w_user", [P, HID])
        b_item = sb("b_item", [P, HID])
        b_tail = sb("b_tail", [P, HID])
        ident = sb("ident", [P, P])
        mask = sb("mask", [P, 1])
        eps = sb("eps", [P, 1])
        stats = sb("stats", [P, XG, 6])
        mean_var = sb("mean_var", [P, XG, 2])
        std = sb("std", [P, XG])
        rstd = sb("rstd", [P, XG])

        def bank(name):
            return ctx.enter_context(nc.psum_tensor(name, [P, 512], F32))

        sums = [bank(f"sums{b}") for b in range(BANKS)]
        x_t_ps = bank("x_t_ps")
        normal_t_ps = bank("normal_t_ps")
        h_ps = [bank(f"h_ps{e}") for e in range(2)]

        weights_in = sem("weights_in")
        late_in = sem("late_in")
        item_in = [sem(f"item_in{e}") for e in range(2)]
        a_in = [sem(f"a_in{s}") for s in range(A_SLOTS)]
        xr_in = [sem(f"xr_in{e}") for e in range(2)]
        tail_in = [sem(f"tail_in{e}") for e in range(2)]
        out_stored = sem("out_stored")
        h_multiplied = sem("h_multiplied")
        h_summed = sem("h_summed")
        h_high_done = sem("h_high_done")
        h_low_done = sem("h_low_done")
        constants_set = sem("constants_set")
        high_done = sem("high_done")
        low_done = sem("low_done")
        tile_used = sem("tile_used")
        bank_done = sem("bank_done")
        bank_free = [sem(f"bank_free{b}") for b in range(BANKS)]
        stats_done = sem("stats_done")
        moments_done = sem("moments_done")
        std_done = sem("std_done")
        rstd_done = sem("rstd_done")
        x_t_done = sem("x_t_done")
        x_t_copied = sem("x_t_copied")
        normal_done = sem("normal_done")
        normal_t_done = [sem(f"normal_t_done{e}") for e in range(2)]
        user_done = sem("user_done")
        tail_high_done = sem("tail_high_done")
        tail_low_done = [sem(f"tail_low_done{e}") for e in range(2)]
        tail_used = [sem(f"tail_used{e}") for e in range(2)]

        WEIGHTS, LATE = 5, 2
        block = ctx.enter_context(nc.Block())

        def columns(ring, s):
            return ring[:, s * BLOCK:(s + 1) * BLOCK]

        def halves(eng, first, section_pair):
            if first:
                for half in range(BANKS // 2):
                    section_pair(half)
            else:
                with eng.Fori(0, BANKS // 2) as half:
                    section_pair(half)

        @block.sync
        def _(sp):
            def load_item(c):
                sp.dma_start(item_t[:, c % 2, :],
                             item_cols[:, c * HC * P:(c + 1) * HC * P]).then_inc(item_in[c % 2], 16)

            def load_tile(tile, s):
                sp.dma_start(columns(a_ring, s), adj_main[bass.ds(tile * P, P), :]).then_inc(a_in[s], 16)

            def load_first_tiles(t0, count):
                for t in range(t0, t0 + count):
                    c = t // HC + 1
                    if t % HC == 0 and 2 <= c < H_CHUNKS:
                        sp.wait_ge(h_multiplied, c)
                        load_item(c)
                    if t >= A_SLOTS:
                        sp.wait_ge(low_done, t - A_SLOTS + 1)
                    load_tile(t, t % A_SLOTS)

            def load_tiles(tile, slots):
                for s in slots:
                    sp.wait_ge(low_done, tile + (s - A_SLOTS + 1))
                    load_tile(tile + s, s)

            def load_chunk(n, q, first):
                e, use = q % 2, 2 * n + q // 2
                if not first or q >= 2:
                    sp.wait_ge(normal_t_done[e], use)
                sp.dma_start(xr[:, e, :], x_rows[bass.ds((n * BANKS + q) * P, P), :]).then_inc(xr_in[e], 16)
                if not first or q >= 2:
                    sp.wait_ge(tail_low_done[e], use)
                sp.dma_start(tail_raw[:, e, :],
                             adj_tail[bass.ds((n * BANKS + q) * TAIL, TAIL), :]).then_inc(tail_in[e], 16)

            def load_block(n):
                tile = TILES * n
                load_tiles(tile, range(A_SLOTS))
                for q in range(BANKS):
                    load_chunk(n, q, False)
                    group = tile + A_SLOTS + q * SECTION
                    if q == 0:
                        load_tiles(group, range(3))
                        sp.wait_ge(bank_free[BANKS - 1], n)
                        sp.dma_start(out[bass.ds((n - 1) * P, P), :], xo[:, :]).then_inc(out_stored, 16)
                        load_tiles(group, range(3, A_SLOTS))
                    else:
                        load_tiles(group, range(A_SLOTS))
                    with sp.Fori(1, SECTION // A_SLOTS) as k:
                        load_tiles(group + k * A_SLOTS, range(A_SLOTS))

            sp.dma_start(w_item[:, :], w_item_t).then_inc(weights_in, 16)
            sp.dma_start(item_tail_t[:, :], item_tail_cols).then_inc(weights_in, 16)
            sp.dma_start(b_tail[:, :], b_tail_rows).then_inc(weights_in, 16)
            sp.dma_start(b_item[:, :], b_item_rows).then_inc(weights_in, 16)
            sp.dma_start(mask[:, :], split_mask).then_inc(weights_in, 16)
            load_item(0)
            load_item(1)
            load_first_tiles(0, 2)
            sp.dma_start(w_user[:, :], w_user_t).then_inc(late_in, 16)
            sp.dma_start(ident[:, :], identity).then_inc(late_in, 16)
            load_first_tiles(2, A_SLOTS - 2)
            for q in range(BANKS):
                load_chunk(0, q, True)
                load_first_tiles(A_SLOTS + q * SECTION, SECTION)
            with sp.Fori(1, BLOCKS) as n:
                load_block(n)
            for b in range(BANKS):
                sp.wait_ge(bank_free[b], BLOCKS)
                sp.dma_start(out[(BLOCKS - 1) * P:BLOCKS * P, b * BANK:(b + 1) * BANK],
                             xo[:, b * BANK:(b + 1) * BANK]).then_inc(out_stored, 16)
            sp.wait_ge(out_stored, (BLOCKS - 1 + BANKS) * 16)

        @block.scalar
        def _(act):
            def high_h(c):
                act.wait_ge(h_summed, c + 2)
                nc.scalar.activation(h_high[:, c * HC * HID:(c + 1) * HC * HID], h_sum[:, c % 2, :],
                                     ACT.Copy).then_inc(h_high_done, 1)

            def high_tile(loads, used, j):
                s, r = j % A_SLOTS, j % PART_SLOTS
                act.wait_ge(a_in[s], loads * 16)
                if used is not None:
                    act.wait_ge(tile_used, used)
                nc.scalar.activation(columns(high_ring, r), columns(a_ring, s), ACT.Copy).then_inc(high_done, 1)

            def high_tiles(n, group, count, first):
                for j in range(count):
                    used = n * TILES + group * A_SLOTS + (j - PART_SLOTS + 1)
                    if first and used <= 0:
                        used = None
                    high_tile(n * (TILES // A_SLOTS) + group + (j // A_SLOTS + 1), used, j)
                    if first and j % HC == 0:
                        c = (group * A_SLOTS + j) // HC + 1
                        if c < H_CHUNKS:
                            high_h(c)

            def high_block(n, first=False):
                high_tiles(n, 0, A_SLOTS, first)

                def section_pair(half):
                    for e in range(2):
                        use = 2 * n + half
                        chunk = BANKS * n + 2 * half + e
                        group = 6 * half + (1 + 3 * e)
                        act.wait_ge(tail_in[e], (use + 1) * 16)
                        if not (first and half == 0):
                            act.wait_ge(tail_used[e], use)
                        for p in STACK[0::2]:
                            last = nc.scalar.activation(tail_moving[p:p + TAIL, e, :], tail_raw[:, e, :], ACT.Copy)
                        last.then_inc(tail_high_done, 1)
                        high_tiles(n, group, A_SLOTS, first)
                        act.wait_ge(moments_done, chunk + 1)
                        nc.scalar.activation(std[:, :], mean_var[:, :, 1], ACT.Sqrt,
                                             bias=eps[:, 0:1]).then_inc(std_done, 1)
                        high_tiles(n, group + 1, A_SLOTS, first)
                        act.wait_ge(x_t_done, chunk + 1)
                        if not first:
                            act.wait_ge(out_stored, n * 16)
                        nc.scalar.activation(xo[:, bass.ds((2 * half + e) * BANK, BANK)], x_t_ps[:, 0:BANK],
                                             ACT.Copy).then_inc(x_t_copied, 1)
                        act.wait_ge(normal_t_done[e], use + 1)
                        nc.scalar.activation(user_t[:, e, :], normal_t_ps[:, :], ACT.Relu).then_inc(user_done, 1)
                        high_tiles(n, group + 2, A_SLOTS, first)

                halves(act, first, section_pair)

            act.wait_ge(constants_set, 1)
            act.wait_ge(h_summed, 1)
            nc.scalar.activation(tail_weights[:, :], tail_sum[:, :], ACT.Copy).then_inc(h_high_done, 1)
            high_h(0)
            high_block(0, first=True)
            with act.Fori(1, BLOCKS) as n:
                high_block(n)

        @block.vector
        def _(dve):
            b_wide = b_item[:, :].unsqueeze(1).to_broadcast([P, HC, HID])

            def add_bias(c):
                if c >= 2:
                    dve.wait_ge(h_low_done, c)
                dve.wait_ge(h_multiplied, c + 2)
                nc.vector.tensor_tensor(h_sum[:, c % 2, :].rearrange("p (t h) -> p t h", t=HC),
                                        h_ps[(c + 1) % 2][:, 0:HC * HID].rearrange("p (t h) -> p t h", t=HC),
                                        b_wide, ALU.add).then_inc(h_summed, 1)

            def low_h(c):
                dve.wait_ge(h_high_done, c + 2)
                h = slice(c * HC * HID, (c + 1) * HC * HID)
                nc.vector.tensor_tensor(h_low[:, h], h_sum[:, c % 2, :], h_high[:, h].bitcast(F32),
                                        ALU.subtract).then_inc(h_low_done, 1)

            def low_tile(n, group, j, first):
                c = (group * A_SLOTS + j) // HC + 1 if first else H_CHUNKS
                if j % HC == 0 and c < H_CHUNKS:
                    add_bias(c)
                dve.wait_ge(high_done, n * TILES + group * A_SLOTS + (j + 1))
                nc.vector.tensor_tensor(columns(low_ring, j % PART_SLOTS), columns(a_ring, j % A_SLOTS),
                                        columns(high_ring, j % PART_SLOTS).bitcast(F32),
                                        ALU.subtract).then_inc(low_done, 1)
                if j % HC == 1 and c < H_CHUNKS:
                    low_h(c)

            def finish_bank(n, b):
                if b < BANKS - 1:
                    dve.wait_ge(bank_done, n * (BANKS - 1) + (b - BANKS + 2))
                else:
                    dve.wait_ge(tile_used, n * TILES)
                dve.wait_ge(x_t_copied, n * BANKS)
                nc.vector.scalar_tensor_tensor(out=xo[:, b * BANK:(b + 1) * BANK], in0=sums[b][:, 0:BANK],
                                               scalar=0.0, in1=xo[:, b * BANK:(b + 1) * BANK], op0=ALU.max,
                                               op1=ALU.add).then_inc(bank_free[b], 1)

            def low_block(n, first=False):
                for j in range(A_SLOTS):
                    low_tile(n, 0, j, first)
                    if j == 1 and not first:
                        for b in range(BANKS):
                            finish_bank(n, b)

                def section_pair(half):
                    for e in range(2):
                        use = 2 * n + half
                        chunk = BANKS * n + 2 * half + e
                        group = 6 * half + (1 + 3 * e)
                        dve.wait_ge(xr_in[e], (use + 1) * 16)
                        for g in range(XG):
                            last = nc.vector.bn_stats(stats[:, g, :], xr[:, e, g * HID:(g + 1) * HID])
                        last.then_inc(stats_done, 1)
                        dve.wait_ge(stats_done, chunk + 1)
                        low_tile(n, group, 0, first)
                        for g in range(XG):
                            last = nc.vector.bn_aggr(mean_var[:, g, :], stats[:, g, :])
                        last.then_inc(moments_done, 1)
                        for j in range(1, A_SLOTS):
                            low_tile(n, group, j, first)
                        dve.wait_ge(std_done, chunk + 1)
                        nc.vector.reciprocal(rstd[:, :], std[:, :]).then_inc(rstd_done, 1)
                        dve.wait_ge(tail_high_done, chunk + 1)
                        for p in STACK[1::2]:
                            last = nc.vector.tensor_tensor(tail_moving[p:p + TAIL, e, :], tail_raw[:, e, :],
                                                           tail_moving[0:TAIL, e, :].bitcast(F32), ALU.subtract)
                        last.then_inc(tail_low_done[e], 1)
                        dve.wait_ge(rstd_done, chunk + 1)
                        dve.wait_ge(x_t_done, chunk + 1)
                        for g in range(XG):
                            rows = xr[:, e, g * HID:(g + 1) * HID]
                            last = nc.vector.tensor_scalar(rows, rows, mean_var[:, g, 0:1], rstd[:, g:g + 1],
                                                           ALU.subtract, ALU.mult)
                        last.then_inc(normal_done, 1)
                        for j in range(A_SLOTS):
                            low_tile(n, group + 1, j, first)
                        for j in range(A_SLOTS):
                            low_tile(n, group + 2, j, first)

                halves(dve, first, section_pair)

            nc.vector.memset(eps[:, :], EPS)
            nc.vector.memset(tail_moving[:, :, :].bitcast(F32), 1.0).then_inc(constants_set, 1)
            dve.wait_ge(weights_in, WEIGHTS * 16)
            dve.wait_ge(h_multiplied, 1)
            nc.vector.tensor_tensor(tail_sum[:, :], h_ps[0][:, 0:HID], b_tail[:, :], ALU.add).then_inc(h_summed, 1)
            add_bias(0)
            dve.wait_ge(h_high_done, 1)
            nc.vector.scalar_tensor_tensor(out=tail_weights[:, :], in0=tail_weights[:, :].bitcast(F32),
                                           scalar=mask[:, 0:1], in1=tail_sum[:, :], op0=ALU.mult,
                                           op1=ALU.add).then_inc(h_low_done, 1)
            low_h(0)
            low_block(0, first=True)
            with dve.Fori(1, BLOCKS) as n:
                low_block(n)
            for b in range(BANKS):
                finish_bank(BLOCKS, b)

        @block.tensor
        def _(pe):
            def multiply_h(c):
                if c >= 1:
                    pe.wait_ge(h_summed, c)
                pe.wait_ge(item_in[c % 2], (c // 2 + 1) * 16)
                for k in range(HC):
                    last = nc.tensor.matmul(h_ps[(c + 1) % 2][:, k * HID:(k + 1) * HID],
                                            item_t[:, c % 2, k * P:(k + 1) * P], w_item[:, :],
                                            start=True, stop=True)
                last.then_inc(h_multiplied, 1)

            def product(t, weights, ring, b, start=False, stop=False):
                r = t % PART_SLOTS
                return nc.tensor.matmul(sums[b][:, 0:BANK], weights[:, t * HID:(t + 1) * HID],
                                        ring[:, r * BLOCK + b * BANK:r * BLOCK + (b + 1) * BANK],
                                        start=start, stop=stop)

            def transpose_rows(e, to):
                for g in range(XG):
                    last = nc.tensor.transpose(to[:, g * P:(g + 1) * P], xr[:, e, g * HID:(g + 1) * HID],
                                               ident[:, :])
                return last

            def multiply_block(n, first=False):
                for t in range(TILES):
                    q, at = divmod(t - A_SLOTS, SECTION)
                    e = q % 2
                    if at == 0:
                        pe.wait_ge(xr_in[e], (n * 2 + (q // 2 + 1)) * 16)
                        if not first or q > 0:
                            pe.wait_ge(x_t_copied, n * BANKS + q)
                        transpose_rows(e, x_t_ps).then_inc(x_t_done, 1)
                    if q >= 0 and at == A_SLOTS:
                        pe.wait_ge(normal_done, n * BANKS + (q + 1))
                        transpose_rows(e, normal_t_ps).then_inc(normal_t_done[e], 1)
                    if q >= 0 and at == 2 * A_SLOTS + PART_SLOTS:
                        pe.wait_ge(user_done, n * BANKS + (q + 1))
                        nc.tensor.matmul(sums[q][:, 0:BANK], w_user[:, :], user_t[:, e, 0:BANK],
                                         start=False, stop=False)
                        pe.wait_ge(tail_low_done[e], n * 2 + (q // 2 + 1))
                        nc.tensor.matmul(sums[q][:, 0:BANK], tail_weights[:, :], tail_moving[:, e, :],
                                         start=False, stop=False).then_inc(tail_used[e], 1)
                    if first and t % HC == 0:
                        if t // HC + 2 < H_CHUNKS:
                            multiply_h(t // HC + 2)
                        pe.wait_ge(h_low_done, t // HC + 2)
                    pe.wait_ge(low_done, n * TILES + (t + 1))
                    if t < TILES - 1:
                        for b in range(BANKS):
                            if t == 0 and not first:
                                pe.wait_ge(bank_free[b], n)
                            product(t, h_high, high_ring, b, start=(t == 0))
                        for b in range(BANKS):
                            product(t, h_high, low_ring, b)
                        for b in range(BANKS):
                            last = product(t, h_low, high_ring, b)
                        last.then_inc(tile_used, 1)
                    else:
                        for b in range(BANKS):
                            product(t, h_high, high_ring, b)
                            product(t, h_high, low_ring, b)
                            last = product(t, h_low, high_ring, b, stop=True)
                            last.then_inc(bank_done if b < BANKS - 1 else tile_used, 1)

            pe.wait_ge(weights_in, WEIGHTS * 16)
            nc.tensor.matmul(h_ps[0][:, 0:HID], item_tail_t[:, :], w_item[:, :],
                             start=True, stop=True).then_inc(h_multiplied, 1)
            multiply_h(0)
            multiply_h(1)
            pe.wait_ge(late_in, LATE * 16)
            multiply_block(0, first=True)
            with pe.Fori(1, BLOCKS) as n:
                multiply_block(n)


def kernel(x, adj, L0_gnn_item_feat, L0_gnn_W_item, L0_gnn_b_item, L0_gnn_W_user, L0_gnn_b_user):
    import numpy as np
    import concourse.bacc as bacc
    from concourse.bass_utils import run_bass_kernel_spmd

    f = np.float32
    x, adj, item, wi, bi, wu, bu = (np.asarray(a) for a in (
        x, adj, L0_gnn_item_feat, L0_gnn_W_item, L0_gnn_b_item, L0_gnn_W_user, L0_gnn_b_user))
    whole = TILES * P
    adj_t = adj.T
    adj_main = np.empty((BLOCKS, TILES, P, BLOCK), f)
    for n in range(BLOCKS):
        adj_main[n] = adj_t[:whole, n * BLOCK:(n + 1) * BLOCK].reshape(TILES, P, BLOCK)
    adj_tail = adj_t[whole:].reshape(TAIL, CHUNKS, BANK).transpose(1, 0, 2)
    rows = np.zeros((CHUNKS, XG * P, HID), f)
    rows[:, :BANK] = x.reshape(CHUNKS, BANK, HID)
    item_tail = np.zeros((HID, P), f)
    b_tail = np.zeros((P, HID), f)
    for p in STACK:
        item_tail[:, p:p + TAIL] = item.T[:, whole:]
        b_tail[p:p + TAIL] = bi
    b_tail[BIAS:BIAS + 2] = bu
    mask = np.zeros((P, 1), f)
    mask[STACK[2]:BIAS] = mask[BIAS + 1] = -1
    arrays = {
        "adj_main": adj_main.reshape(BLOCKS * TILES * P, BLOCK),
        "adj_tail": adj_tail.reshape(CHUNKS * TAIL, BANK),
        "x_rows": rows.reshape(CHUNKS, XG, P, HID).transpose(0, 2, 1, 3).reshape(CHUNKS * P, XG * HID),
        "item_cols": item.T[:, :whole],
        "item_tail_cols": item_tail,
        "w_item_t": wi.T, "w_user_t": wu.T,
        "b_item_rows": np.tile(bi, (P, 1)), "b_tail_rows": b_tail,
        "identity": np.eye(P, dtype=f), "split_mask": mask,
    }
    arrays = {k: np.ascontiguousarray(v) for k, v in arrays.items()}
    nc = bacc.Bacc("TRN2", target_bir_lowering=False, num_devices=1)
    args = [nc.dram_tensor(k, v.shape, mybir.dt.from_np(v.dtype), kind="ExternalInput").ap()
            for k, v in arrays.items()]
    out = nc.dram_tensor("out", (BLOCKS * HID, BLOCK), F32, kind="ExternalOutput").ap()
    build(nc, *args, out)
    r = run_bass_kernel_spmd(nc, [arrays], core_ids=[0])
    return np.ascontiguousarray(
        r.results[0]["out"].reshape(BLOCKS, HID, BLOCK).transpose(0, 2, 1).reshape(N_USER, HID))
```
